# Optimizing a Trainium2 kernel written in Bass

```python
import numpy as np
import jax
import jax.numpy as jnp

def _softmax(x, axis=-1):
    return jax.nn.softmax(x, axis=axis)

def _gelu(x):
    return jax.nn.gelu(x, approximate=True)

def _silu(x):
    return jax.nn.silu(x)

def _sigmoid(x):
    return jax.nn.sigmoid(x)

def _layernorm(x, axis=-1, eps=1e-05):
    m = jnp.mean(x, axis=axis, keepdims=True)
    v = jnp.var(x, axis=axis, keepdims=True)
    return (x - m) / jnp.sqrt(v + eps)

def _scatter_add(tgt, idx, src, axis=0):
    return tgt.at[idx].add(src)

def _segment_sum(src, seg, n):
    return jax.ops.segment_sum(src, seg, n)
kernel_name = 'mk_lm_tower_d1_tok_ids1024_r4_1a19a5'

def setup_inputs(seed: int=0):
    np.random.seed(seed)
    _w = jnp.asarray

    def _rec_inputs():
        import jax
        import jax.numpy as jnp
        _rk = jax.random.key(seed)
        x = jax.random.randint(jax.random.fold_in(_rk, 1), (32, 128), 0, 28, jnp.int32)
        mask_BS_i1_0 = jnp.where(jnp.ones((32, 128), dtype=bool), 1, 0).astype(jnp.int32)
        return (x, mask_BS_i1_0)
    x, mask_BS_i1_0 = _rec_inputs()

    def _L0_tok_setup():
        import jax, jax.numpy as jnp
        import numpy as np
        WINDOW_SIZE = 3
        LN_EPS = 1e-05

        def _sliding_window_features(base_pca, mask_f):
            B, S, F = base_pca.shape
            h = WINDOW_SIZE // 2
            idx = jnp.arange(S)
            start = jnp.maximum(idx - h, 0)
            end = jnp.minimum(idx + h + 1, S)
            masked = base_pca * mask_f[..., None]
            csum = jnp.pad(jnp.cumsum(masked, axis=1), ((0, 0), (1, 0), (0, 0)))
            wsum = csum[:, end, :] - csum[:, start, :]
            mcs = jnp.pad(jnp.cumsum(mask_f, axis=1), ((0, 0), (1, 0)))
            lengths = jnp.maximum(mcs[:, end] - mcs[:, start], 1.0)
            return wsum / lengths[..., None]
        key = jax.random.key(seed)
        ks = jax.random.split(key, 8)
        B, S, V, E = (8, 1024, 28, 256)
        input_ids = jax.random.randint(ks[0], (B, S), 0, V, dtype=jnp.int64)
        attention_mask = jnp.ones((B, S), dtype=jnp.int32)
        emb = jax.random.normal(ks[1], (V, E), dtype=jnp.float32) * 0.02
        emb = emb.at[0].set(0.0)
        pca_lookup = jax.random.normal(ks[2], (V, 20), dtype=jnp.float32)
        proj_w = jax.random.normal(ks[3], (20, E), dtype=jnp.float32) * 0.2
        proj_b = jnp.zeros((E,), dtype=jnp.float32)
        fus_w = jax.random.normal(ks[4], (2 * E, E), dtype=jnp.float32) * 0.02
        fus_b = jnp.zeros((E,), dtype=jnp.float32)
        ln_g = jnp.ones((E,), dtype=jnp.float32)
        ln_b = jnp.zeros((E,), dtype=jnp.float32)
        return {'input_ids': input_ids, 'attention_mask': attention_mask, 'emb': emb, 'pca_lookup': pca_lookup, 'proj_w': proj_w, 'proj_b': proj_b, 'fus_w': fus_w, 'fus_b': fus_b, 'ln_g': ln_g, 'ln_b': ln_b}
    _L0_tok_all = _L0_tok_setup()
    _L0_tok_in = {k: v for k, v in _L0_tok_all.items() if k in ('emb', 'pca_lookup', 'proj_w', 'proj_b', 'fus_w', 'fus_b', 'ln_g', 'ln_b')}
    del _L0_tok_all

    def _L0_attn_setup():
        import jax, jax.numpy as jnp
        import numpy as np
        B, S, D = (4, 512, 256)
        H, K = (16, 64)
        EPS = 0.001
        key = jax.random.key(seed)
        ks = jax.random.split(key, 11)
        s = 0.02
        return {'x': jax.random.normal(ks[0], (B, S, D), jnp.float32), 'Wq': jax.random.normal(ks[1], (D, H, K), jnp.float32) * s, 'bq': jnp.zeros((H, K), jnp.float32), 'Wk': jax.random.normal(ks[2], (D, H, K), jnp.float32) * s, 'bk': jnp.zeros((H, K), jnp.float32), 'Wv': jax.random.normal(ks[3], (D, H, K), jnp.float32) * s, 'bv': jnp.zeros((H, K), jnp.float32), 'Wo': jax.random.normal(ks[4], (H, K, D), jnp.float32) * s, 'bo': jnp.zeros((D,), jnp.float32), 'gamma': jnp.ones((D,), jnp.float32), 'beta': jnp.zeros((D,), jnp.float32)}
    _L0_attn_all = _L0_attn_setup()
    _L0_attn_in = {k: v for k, v in _L0_attn_all.items() if k in ('Wq', 'bq', 'Wk', 'bk', 'Wv', 'bv', 'Wo', 'bo', 'gamma', 'beta')}
    del _L0_attn_all

    def _L0_ffn_setup():
        import jax, jax.numpy as jnp
        import numpy as np
        N_EXPERTS = 16
        TOPK = 2
        CAPACITY_FACTOR = 1.0
        EPS_GATE = 1e-06
        LN_EPS = 1e-05
        key = jax.random.key(seed)
        ks = jax.random.split(key, 8)
        B, S, D, F, E = (4, 512, 256, 1024, N_EXPERTS)
        Fp = F // E
        s = 0.02
        return {'x': jax.random.normal(ks[0], (B, S, D), dtype=jnp.float32), 'wg': s * jax.random.normal(ks[1], (D, E), dtype=jnp.float32), 'bg': jnp.zeros((E,), dtype=jnp.float32), 'w1': s * jax.random.normal(ks[2], (E, D, Fp), dtype=jnp.float32), 'b1': jnp.zeros((E, Fp), dtype=jnp.float32), 'w2': s * jax.random.normal(ks[3], (E, Fp, D), dtype=jnp.float32), 'b2': jnp.zeros((E, D), dtype=jnp.float32), 'gamma': jnp.ones((D,), dtype=jnp.float32), 'beta': jnp.zeros((D,), dtype=jnp.float32)}
    _L0_ffn_all = _L0_ffn_setup()
    _L0_ffn_in = {k: v for k, v in _L0_ffn_all.items() if k in ('wg', 'bg', 'w1', 'b1', 'w2', 'b2', 'gamma', 'beta')}
    del _L0_ffn_all
    return {'x': x, 'mask_BS_i1_0': mask_BS_i1_0, 'L0_tok_emb': _L0_tok_in['emb'], 'L0_tok_pca_lookup': _L0_tok_in['pca_lookup'], 'L0_tok_proj_w': _L0_tok_in['proj_w'], 'L0_tok_proj_b': _L0_tok_in['proj_b'], 'L0_tok_fus_w': _L0_tok_in['fus_w'], 'L0_tok_fus_b': _L0_tok_in['fus_b'], 'L0_tok_ln_g': _L0_tok_in['ln_g'], 'L0_tok_ln_b': _L0_tok_in['ln_b'], 'L0_attn_Wq': _L0_attn_in['Wq'], 'L0_attn_bq': _L0_attn_in['bq'], 'L0_attn_Wk': _L0_attn_in['Wk'], 'L0_attn_bk': _L0_attn_in['bk'], 'L0_attn_Wv': _L0_attn_in['Wv'], 'L0_attn_bv': _L0_attn_in['bv'], 'L0_attn_Wo': _L0_attn_in['Wo'], 'L0_attn_bo': _L0_attn_in['bo'], 'L0_attn_gamma': _L0_attn_in['gamma'], 'L0_attn_beta': _L0_attn_in['beta'], 'L0_ffn_wg': _L0_ffn_in['wg'], 'L0_ffn_bg': _L0_ffn_in['bg'], 'L0_ffn_w1': _L0_ffn_in['w1'], 'L0_ffn_b1': _L0_ffn_in['b1'], 'L0_ffn_w2': _L0_ffn_in['w2'], 'L0_ffn_b2': _L0_ffn_in['b2'], 'L0_ffn_gamma': _L0_ffn_in['gamma'], 'L0_ffn_beta': _L0_ffn_in['beta']}

def reference(x, mask_BS_i1_0, L0_tok_emb, L0_tok_pca_lookup, L0_tok_proj_w, L0_tok_proj_b, L0_tok_fus_w, L0_tok_fus_b, L0_tok_ln_g, L0_tok_ln_b, L0_attn_Wq, L0_attn_bq, L0_attn_Wk, L0_attn_bk, L0_attn_Wv, L0_attn_bv, L0_attn_Wo, L0_attn_bo, L0_attn_gamma, L0_attn_beta, L0_ffn_wg, L0_ffn_bg, L0_ffn_w1, L0_ffn_b1, L0_ffn_w2, L0_ffn_b2, L0_ffn_gamma, L0_ffn_beta):
    import jax
    import jax.numpy as jnp

    def _L0_tok_ref(input_ids, attention_mask, emb, pca_lookup, proj_w, proj_b, fus_w, fus_b, ln_g, ln_b):
        import jax, jax.numpy as jnp
        import numpy as np
        WINDOW_SIZE = 3
        LN_EPS = 1e-05

        def _sliding_window_features(base_pca, mask_f):
            B, S, F = base_pca.shape
            h = WINDOW_SIZE // 2
            idx = jnp.arange(S)
            start = jnp.maximum(idx - h, 0)
            end = jnp.minimum(idx + h + 1, S)
            masked = base_pca * mask_f[..., None]
            csum = jnp.pad(jnp.cumsum(masked, axis=1), ((0, 0), (1, 0), (0, 0)))
            wsum = csum[:, end, :] - csum[:, start, :]
            mcs = jnp.pad(jnp.cumsum(mask_f, axis=1), ((0, 0), (1, 0)))
            lengths = jnp.maximum(mcs[:, end] - mcs[:, start], 1.0)
            return wsum / lengths[..., None]
        token_embeds = emb[input_ids]
        base_pca = pca_lookup[input_ids]
        pca_feat = _sliding_window_features(base_pca, attention_mask.astype(jnp.float32))
        cont = pca_feat @ proj_w + proj_b
        combined = jnp.concatenate([token_embeds, cont], axis=-1)
        fused = combined @ fus_w + fus_b
        mu = jnp.mean(fused, axis=-1, keepdims=True)
        var = jnp.mean(jnp.square(fused - mu), axis=-1, keepdims=True)
        return (fused - mu) * jax.lax.rsqrt(var + LN_EPS) * ln_g + ln_b

    def _L0_attn_ref(x, Wq, bq, Wk, bk, Wv, bv, Wo, bo, gamma, beta):
        import jax, jax.numpy as jnp
        import numpy as np
        B, S, D = (4, 512, 256)
        H, K = (16, 64)
        EPS = 0.001
        q = jnp.einsum('bsd,dhk->bshk', x, Wq) + bq
        k = jnp.einsum('bsd,dhk->bshk', x, Wk) + bk
        v = jnp.einsum('bsd,dhk->bshk', x, Wv) + bv
        scale = 1.0 / jnp.sqrt(jnp.asarray(K, x.dtype))
        scores = jnp.einsum('bqhk,bshk->bhqs', q, k) * scale
        attn = jax.nn.softmax(scores, axis=-1)
        ctx = jnp.einsum('bhqs,bshk->bqhk', attn, v)
        attn_out = jnp.einsum('bqhk,hkd->bqd', ctx, Wo) + bo
        y = x + attn_out
        mu = jnp.mean(y, axis=-1, keepdims=True)
        var = jnp.mean(jnp.square(y - mu), axis=-1, keepdims=True)
        return (y - mu) * jax.lax.rsqrt(var + EPS) * gamma + beta

    def _L0_ffn_ref(x, wg, bg, w1, b1, w2, b2, gamma, beta):
        import jax, jax.numpy as jnp
        import numpy as np
        N_EXPERTS = 16
        TOPK = 2
        CAPACITY_FACTOR = 1.0
        EPS_GATE = 1e-06
        LN_EPS = 1e-05
        B, S, D = x.shape
        E = wg.shape[1]
        capacity = int(CAPACITY_FACTOR * B)
        scores = jax.nn.softmax(x @ wg + bg, axis=-1)
        _, top_i = jax.lax.top_k(scores, TOPK)
        mask = jax.nn.one_hot(top_i, E, dtype=scores.dtype).sum(-2)
        masked = scores * mask
        denom = masked.sum(0, keepdims=True) + EPS_GATE
        route = masked / denom * capacity
        route_e = jnp.transpose(route, (2, 0, 1))
        max_len = S // 2
        _, seq_ids = jax.lax.top_k(route_e, max_len)
        seq_ids = jnp.sort(seq_ids, axis=-1)
        b_idx = jnp.arange(B)[None, :, None]
        xg = x[b_idx, seq_ids]
        h = jnp.einsum('ebld,edf->eblf', xg, w1) + b1[:, None, None, :]
        h = jax.nn.gelu(h, approximate=False)
        out = jnp.einsum('eblf,efd->ebld', h, w2) + b2[:, None, None, :]
        outs = jnp.zeros_like(x).at[b_idx, seq_ids].add(out)
        z = x + outs
        mu = z.mean(-1, keepdims=True)
        var = ((z - mu) ** 2).mean(-1, keepdims=True)
        return (z - mu) / jnp.sqrt(var + LN_EPS) * gamma + beta
    h = _L0_tok_ref(x, mask_BS_i1_0, L0_tok_emb, L0_tok_pca_lookup, L0_tok_proj_w, L0_tok_proj_b, L0_tok_fus_w, L0_tok_fus_b, L0_tok_ln_g, L0_tok_ln_b)
    h = h + _L0_attn_ref(_layernorm(h, axis=-1), L0_attn_Wq, L0_attn_bq, L0_attn_Wk, L0_attn_bk, L0_attn_Wv, L0_attn_bv, L0_attn_Wo, L0_attn_bo, L0_attn_gamma, L0_attn_beta)
    h = h + _L0_ffn_ref(_layernorm(h, axis=-1), L0_ffn_wg, L0_ffn_bg, L0_ffn_w1, L0_ffn_b1, L0_ffn_w2, L0_ffn_b2, L0_ffn_gamma, L0_ffn_beta)
    return h

_drawn_inputs = setup_inputs


def setup_inputs(seed=0):
    import zlib

    import numpy as np

    out = dict(_drawn_inputs(seed))
    spreads = {'L0_tok_proj_b': (0.0, 0.1),
     'L0_tok_fus_b': (0.0, 0.1),
     'L0_tok_ln_g': (1.0, 0.2),
     'L0_tok_ln_b': (0.0, 0.1),
     'L0_attn_bq': (0.0, 0.8),
     'L0_attn_bk': (0.0, 0.8),
     'L0_attn_bv': (0.0, 0.1),
     'L0_attn_bo': (0.0, 0.1),
     'L0_attn_gamma': (1.0, 0.2),
     'L0_attn_beta': (0.0, 0.1),
     'L0_ffn_bg': (0.0, 0.1),
     'L0_ffn_b1': (0.0, 0.8),
     'L0_ffn_b2': (0.0, 0.1),
     'L0_ffn_gamma': (1.0, 0.2),
     'L0_ffn_beta': (0.0, 0.1)}
    factors = {'L0_attn_Wq': 8.0, 'L0_attn_Wk': 8.0}
    for name, (base, spread) in spreads.items():
        noise = np.random.default_rng([zlib.crc32(name.encode()), seed]).standard_normal(out[name].shape)
        drawn = base * np.exp(spread * noise) if base else spread * noise
        out[name] = jnp.asarray(drawn.astype(out[name].dtype))
    for name, factor in factors.items():
        out[name] = (out[name] * factor).astype(out[name].dtype)
    return out
```

```python
from contextlib import ExitStack

import numpy as np

import concourse.bass as bass
from concourse import mybir

F32 = mybir.dt.float32
F16 = mybir.dt.float16
I32 = mybir.dt.int32
ALU = mybir.AluOpType
ACT = mybir.ActivationFunctionType
AX = mybir.AxisListType

P = 128
B, S, D = 32, 128, 256
V = 28
H, K = 16, 64
E, FP = 16, 64
KC = D // P
HD = H * K // P
NJ = E * FP // P
UD = 64
R2, ONE, SHIFT = 2 * V, 2 * V + 1, 2 * V + 2
GB = 4
NG = B // GB
TAKE = S // 2

T_SCALE = 16.0
G_SCALE = 16.0
Y_SCALE = 16.0
W_SCALE = 64.0
X_SCALE = 64.0
MASK_BIG = 32768.0

INPUTS = {
    "idsT": ([P, B], I32), "maskT": ([P, B], I32),
    "embT": ([P, KC, V], F32), "pcaT": ([20, V], F32), "proj_w": ([20, D], F32), "proj_bT": ([P, KC], F32),
    "fus_w": ([P, 2 * KC, D], F32), "fus_b": ([1, D], F32), "ln_g": ([1, D], F32), "ln_b": ([1, D], F32),
    "wq": ([P, KC, H * K], F32), "wk": ([P, KC, H * K], F32), "wv": ([P, KC, H * K], F32),
    "wo": ([P, HD, D], F32), "bqT": ([P, HD], F32), "bkT": ([P, HD], F32), "bvT": ([P, HD], F32),
    "bo": ([1, D], F32), "gamma1": ([1, D], F32), "beta1": ([1, D], F32),
    "wg": ([P, KC, E], F32), "bg": ([1, E], F32),
    "w1": ([P, KC, E * FP], F32), "b1T": ([P, NJ], F32), "w2": ([P, NJ, D], F32), "b2": ([E, D], F32),
    "gamma2": ([1, D], F32), "beta2": ([1, D], F32),
    "ident": ([P, P], F32), "band": ([P, P], F32), "iota": ([P, V], F32), "countdown": ([P, E], F32),
    "expert_of": ([P, NJ, P], F16),
}


class At:

    def __init__(self, pair, off):
        self.pair, self.off, self.par = pair, off, off % 2

    def plus(self, n):
        return At(self.pair, self.off + n)

    def val(self, times=1, add=0):
        return self.pair * (2 * times) + (times * self.off + add)

    def half(self, times=1, add=0):
        return self.pair * times + (times * (self.off // 2) + add)

    def from_(self, n):
        return not isinstance(self.pair, int) or 2 * self.pair + self.off >= n


def build(nc, d, out):
    with ExitStack() as ctx:
        def sb(name, shape, dt=F32, scope=ctx):
            return scope.enter_context(nc.sbuf_tensor("s_" + name, shape, dt))

        def sem(name):
            return ctx.enter_context(nc.semaphore(name))

        tok = sb("h", [P, B, D])
        mvx = sb("mvx", [P, B, 2])
        lg = sb("lg", [P, B, E])
        ident = sb("ident", [P, P])
        g_b, b_b, be1_b, ga1_b, ga2_b, be2_b = (sb(n, [P, D]) for n in ("g_b", "b_b", "be1_b", "ga1_b", "ga2_b", "be2_b"))
        bg_b = sb("bg_b", [P, E])
        w1s = sb("w1s", [P, 2, KC, E * FP], F16)
        w2s = sb("w2s", [P, 2, NJ, D], F16)
        wgs = sb("wgs", [P, 2, KC, E], F16)
        b1T = sb("b1T", [P, NJ])
        b2s = sb("b2s", [P, D], F16)
        expert_of = sb("expert_of", [P, NJ, P], F16)
        mhalf = sb("mhalf", [P, B])
        eps_y, eps_x, eps_z = (sb(n, [P, 1]) for n in ("eps_y", "eps_x", "eps_z"))
        gp = sb("gp", [P, 2, 4, 2, UD], F16)
        z = sb("z", [P, HD, D])
        mr = sb("mr", [P, D], F16)
        ub = sb("ub", [P, B, 2, P], F16)
        uf = sb("uf", [P, B, UD])
        ones = sb("ones", [P, UD])
        psum = [ctx.enter_context(nc.psum_tensor(f"ps{n}", [P, 512], F32)) for n in range(8)]

        met = sem("met")

        def both(t):
            return t.rearrange("p a b -> p (a b)")

        one = ctx.enter_context(ExitStack())

        def sb1(name, shape, dt=F32):
            return sb(name, shape, dt, one)

        stage = sb1("stage", [P, 4, 2048])
        stage2 = sb1("stage2", [P, 2, 2048])
        qkv_t = sb1("qkv_t", [P, 3, HD, UD])
        ids_i, mask_i = sb1("ids_i", [P, B], I32), sb1("mask_i", [P, B], I32)
        ids_f, mask_f = sb1("ids_f", [P, B]), sb1("mask_f", [P, B])
        band, iota = sb1("band", [P, P]), sb1("iota", [P, V])
        lhs_t = sb1("lhs_t", [P, 2 * KC, UD])
        pcaT, proj_w, proj_bT = sb1("pcaT", [20, V]), sb1("proj_w", [20, D]), sb1("proj_bT", [P, KC])
        fus_w, fus_b = sb1("fus_w", [P, 2 * KC, D]), sb1("fus_b", [1, D])
        bT = sb1("bT", [P, 3, HD])
        row1 = sb1("row1", [1, UD])
        wg_f, b2_f = sb1("wg_f", [P, KC, E]), sb1("b2_f", [80, D])
        masked = sb1("masked", [P, B, V + 1])
        cnt_len, share = sb1("cnt_len", [P, B]), sb1("share", [P, B])
        tt = sb1("tt", [UD, 2, D])
        tts = sb1("tts", [P, 2, D], F16)
        mb = sb1("mb", [UD, D])
        mbo = sb1("mbo", [UD, D])
        msum = sb1("msum", [UD, 4])
        mt = sb1("mt", [P, KC, UD])
        stg = sb1("stg", [P, 2, GB, 2, UD])
        ssq, r1 = sb1("ssq", [P, B]), sb1("r1", [P, B])
        var1, var2 = sb1("var1", [P, B]), sb1("var2", [P, B])
        sq = sb1("sq", [P, D])
        ht = sb1("ht", [P, 2, D])
        bst = sb1("bst", [P, 2, 6])
        mvh = sb1("mvh", [P, 2, 2])
        vh = sb1("vh", [P, B])
        r2, r12 = sb1("r2", [P, B]), sb1("r12", [P, B])

        in_tok, in_tab, in_row, in_qkv, in_qk_b, in_wo, in_w12, in_lnb, in_bo, in_b2 = (
            sem(n) for n in ("in_tok", "in_tab", "in_row", "in_qkv", "in_qk_b", "in_wo", "in_w12", "in_lnb", "in_bo",
                             "in_b2"))
        zeroed = sem("zeroed")
        ids_ok, hot_ok, masked_ok = sem("ids_ok"), sem("hot_ok"), sem("masked_ok")
        cnt_ready, len_ok, shares_ok = sem("cnt_ready"), sem("len_ok"), sem("shares_ok")
        pp_ready, lhs_ok, tab_ready = sem("pp_ready"), sem("lhs_ok"), sem("tab_ready")
        tab_step, tts_ok = sem("tab_step"), sem("tts_ok")
        m_ok, mt_ready, mt_ok = sem("m_ok"), sem("mt_ready"), sem("mt_ok")
        mhi_ok = sem("mhi_ok")
        qkv_ready, qkv_ok, g_ready, ghi_ok, glo_ok, z_ready, z_ok = (
            sem(n) for n in ("qkv_ready", "qkv_ok", "g_ready", "ghi_ok", "glo_ok", "z_ready", "z_ok"))
        w_hi = sem("w_hi")
        st_a, t_a, hi_a, lo_a, f_a, sq_a = (sem(n) for n in ("st_a", "t_a", "hi_a", "lo_a", "f_a", "sq_a"))
        var_ok, r1_ok = sem("var_ok"), sem("r1_ok")
        f_b, h_b, bn_b, ag_b, mv_b, tok_b = (sem(n) for n in ("f_b", "h_b", "bn_b", "ag_b", "mv_b", "tok_b"))
        v2_ok, r2_ok, r12_ok, u_ok = sem("v2_ok"), sem("r2_ok"), sem("r12_ok"), sem("u_ok")
        st_c, t_c, hi_c, lo_c = (sem(n) for n in ("st_c", "t_c", "hi_c", "lo_c"))

        stage_w = stage[:].rearrange("p a (c n) -> p a c n", c=KC)
        wo_v = stage[:, 3, :].rearrange("p (c n) -> p c n", c=HD)
        w1_v = stage2[:, 0, :].rearrange("p (c n) -> p c n", c=KC)
        w2_v = stage2[:, 1, :].rearrange("p (c n) -> p c n", c=NJ)
        cnt_ps = [psum[0][:, 0:16 * (V + 1)].rearrange("p (b v) -> p b v", b=16),
                  psum[1][:, 0:16 * (V + 1)].rearrange("p (b v) -> p b v", b=16)]
        uf_g = uf[:].rearrange("p (g f) u -> p g f u", f=GB)
        ub_g = ub[:].rearrange("p (g f) a t -> p g f a t", f=GB)

        G_PARTS = [(hf, ab, m) for hf in range(2) for ab in range(2) for m in range(2)]
        Z_BANKS = [(0, 2), (1, 3), (4, 6), (5, 7)]

        def g_part(hf, ab, m):
            c = (4 * hf + 2 * ab) * UD
            return psum[m][0:UD, c:c + 2 * UD].rearrange("p (t u) -> p t u", t=2)

        with nc.Block() as block:
            @block.sync
            def _(sp):
                sp.dma_start(ids_i[:], d["idsT"]).then_inc(in_tok, 16)
                sp.dma_start(mask_i[:], d["maskT"]).then_inc(in_tok, 16)
                sp.dma_start(iota[:], d["iota"]).then_inc(in_tok, 16)
                sp.dma_start(band[:], d["band"]).then_inc(in_tok, 16)
                sp.dma_start(pcaT[:], d["pcaT"]).then_inc(in_tab, 16)
                sp.dma_start(proj_w[:], d["proj_w"]).then_inc(in_tab, 16)
                sp.dma_start(proj_bT[:], d["proj_bT"]).then_inc(in_tab, 16)
                sp.dma_start(fus_b[:], d["fus_b"]).then_inc(in_tab, 16)
                sp.dma_start(fus_w[:], d["fus_w"]).then_inc(in_tab, 16)
                sp.dma_start(ident[:], d["ident"]).then_inc(in_tab, 16)
                sp.wait_ge(zeroed, 1)
                sp.dma_start(lhs_t[:, 0:KC, 0:V], d["embT"]).then_inc(in_tab, 16)
                for t, name in ((g_b, "ln_g"), (b_b, "ln_b"), (be1_b, "beta1")):
                    sp.dma_start(t[:], d[name].to_broadcast([P, D])).then_inc(in_row, 16)
                sp.wait_ge(zeroed, 2)
                sp.dma_start(mb[R2:R2 + 1, :], d["ln_b"]).then_inc(in_lnb, 16)
                for n, name in enumerate(("wq", "wk", "wv")):
                    sp.dma_start(stage_w[:, n], d[name]).then_inc(in_qkv, 16)
                for n, name in enumerate(("bqT", "bkT", "bvT")):
                    sp.dma_start(bT[:, n, :], d[name]).then_inc(in_qk_b, 16)
                sp.dma_start(wo_v, d["wo"]).then_inc(in_wo, 16)
                sp.wait_ge(m_ok, 1)
                sp.dma_start(mbo[ONE:ONE + 1, :], d["bo"]).then_inc(in_bo, 16)

            @block.gpsimd
            def _(pool):
                nc.gpsimd.memset(lhs_t[:], 0.0).then_inc(zeroed, 1)
                nc.gpsimd.memset(mb[:], 0.0).then_inc(zeroed, 1)
                nc.gpsimd.memset(tt[:], 0.0).then_inc(zeroed, 1)
                nc.gpsimd.memset(uf[:], 0.0).then_inc(zeroed, 1)
                nc.gpsimd.memset(row1[:], 0.0).then_inc(zeroed, 1)
                nc.gpsimd.memset(mhalf[:], -0.5).then_inc(zeroed, 1)
                nc.gpsimd.memset(ones[:], 1.0).then_inc(zeroed, 1)
                nc.gpsimd.memset(b2s[:], 0.0).then_inc(zeroed, 1)
                nc.gpsimd.memset(eps_y[:], 1e-3 * Y_SCALE ** 2)
                nc.gpsimd.memset(eps_x[:], 1e-5)
                nc.gpsimd.memset(eps_z[:], 1e-5 * X_SCALE ** 2)
                pool.wait_ge(zeroed, 8)
                nc.gpsimd.memset(row1[:, 0:V], 1.0).then_inc(zeroed, 1)
                pool.dma_start(w1_v, d["w1"]).then_inc(in_w12, 16)
                pool.dma_start(w2_v, d["w2"]).then_inc(in_w12, 16)
                pool.dma_start(wg_f[:], d["wg"]).then_inc(in_w12, 16)
                pool.dma_start(b2_f[32:48, :], d["b2"]).then_inc(in_b2, 16)
                pool.dma_start(b2_f[64:80, :], d["b2"]).then_inc(in_b2, 16)
                pool.dma_start(b1T[:], d["b1T"]).then_inc(in_b2, 16)
                pool.dma_start(expert_of[:], d["expert_of"]).then_inc(in_b2, 16)
                for t, name in ((ga1_b, "gamma1"), (ga2_b, "gamma2"), (be2_b, "beta2")):
                    pool.dma_start(t[:], d[name].to_broadcast([P, D])).then_inc(in_b2, 16)
                pool.dma_start(bg_b[:], d["bg"].to_broadcast([P, E])).then_inc(in_b2, 16)

                def stage_rows(g, done, sem_out):
                    if g.from_(2):
                        pool.wait_ge(done, g.val(1, -1))
                    for c in range(2):
                        nc.gpsimd.tensor_copy(stg[:, g.par, :, c, :], uf_g[:, g.val()]).then_inc(sem_out, 1)

                pool.wait_ge(shares_ok, 2)
                for g in range(2):
                    stage_rows(At(0, g), t_a, st_a)
                with pool.Fori(0, NG // 2 - 1) as k:
                    for g in range(2, 4):
                        stage_rows(At(k, g), t_a, st_a)
                pool.wait_ge(sq_a, B)
                nc.gpsimd.tensor_scalar(var1[:], ssq[:], 1.0 / D, 1e-5 * T_SCALE ** 2, ALU.mult, ALU.add).then_inc(var_ok, 1)
                pool.wait_ge(var_ok, 1)
                nc.gpsimd.tensor_tensor(r1[:], var1[:], mhalf[:], ALU.pow).then_inc(r1_ok, 1)

                def add_beta(b):
                    pool.wait_ge(h_b, b.val(1, 1))
                    nc.gpsimd.tensor_tensor(tok[:, b.val(), :], ht[:, b.par, :], be1_b[:], ALU.add).then_inc(tok_b, 1)

                pool.wait_ge(in_row, 48)
                with pool.Fori(0, B // 2) as k:
                    for b in range(2):
                        add_beta(At(k, b))
                pool.wait_ge(mv_b, B)
                nc.gpsimd.tensor_scalar(var2[:], vh[:], 1e-5, None, ALU.add).then_inc(v2_ok, 1)
                pool.wait_ge(v2_ok, 1)
                nc.gpsimd.tensor_tensor(r2[:], var2[:], mhalf[:], ALU.pow).then_inc(r2_ok, 1)
                pool.wait_ge(u_ok, 3)
                for g in range(2):
                    stage_rows(At(0, g), t_c, st_c)
                with pool.Fori(0, NG // 2 - 1) as k:
                    for g in range(2, 4):
                        stage_rows(At(k, g), t_c, st_c)

            @block.scalar
            def _(act):
                nc.scalar.preload_act_table(ACT.Exp)
                act.wait_ge(tab_step, 4)
                nc.scalar.activation(both(tts[0:UD]), both(tt[:]), ACT.Copy, scale=T_SCALE).then_inc(tts_ok, 1)

                def hi_part(g, t_sem, out_sem):
                    act.wait_ge(t_sem, g.val(1, 1))
                    nc.scalar.activation(ub_g[:, g.val(), :, 0, :], psum[2 + g.par][:].rearrange("p (f t) -> p f t", f=GB),
                                         ACT.Copy).then_inc(out_sem, 1)

                def squares(b, bank):
                    act.wait_ge(f_a, b.val(1, 1))
                    if b.from_(1):
                        act.wait_ge(sq_a, b.val())
                    nc.scalar.activation(sq[:], psum[bank][:, 0:D], ACT.Square,
                                         accum_out=ssq[:, bass.ds(b.val(), 1)]).then_inc(sq_a, 1)

                def hi_and_squares(g, gb):
                    hi_part(g, t_a, hi_a)
                    for f in range(GB):
                        squares(At(gb, g.off * GB + f), 4 + f)

                hi_and_squares(At(0, 0), 0)
                hi_and_squares(At(0, 1), 0)
                with act.Fori(0, NG // 2 - 1) as k:
                    hi_and_squares(At(k, 2), k * GB)
                    hi_and_squares(At(k, 3), k * GB)
                act.wait_ge(in_bo, 16)
                nc.scalar.activation(mr[0:UD, :], mbo[:], ACT.Copy, scale=Y_SCALE).then_inc(mhi_ok, 1)
                act.wait_ge(g_ready, 2)
                for hf, ab, m in G_PARTS:
                    nc.scalar.activation(gp[0:UD, hf, m::2, ab, :], g_part(hf, ab, m), ACT.Copy,
                                         scale=G_SCALE * K ** -0.5).then_inc(ghi_ok, 1)
                with act.Fori(0, NG // 2) as k:
                    for g in range(2):
                        act.wait_ge(f_b, B)
                        hi_part(At(k, g), t_c, hi_c)

            @block.vector
            def _(dve):
                def bcast(t, n):
                    return t.rearrange("p (b o) -> p b o", o=1).to_broadcast([P, B, n])

                dve.wait_ge(in_tok, 64).then_inc(met, 1)
                nc.vector.tensor_copy(ids_f[:], ids_i[:]).then_inc(ids_ok, 1)
                nc.vector.tensor_copy(mask_f[:], mask_i[:]).then_inc(ids_ok, 1)
                dve.wait_ge(zeroed, 4)
                dve.wait_ge(ids_ok, 2)
                nc.vector.tensor_tensor(uf[:, :, 0:V], iota[:].rearrange("p (o v) -> p o v", o=1).to_broadcast([P, B, V]),
                                        bcast(ids_f[:], V), ALU.is_equal).then_inc(hot_ok, 1)
                nc.vector.tensor_copy(masked[:, :, V:V + 1], mask_f[:].rearrange("p (b o) -> p b o", o=1)).then_inc(masked_ok, 1)
                dve.wait_ge(hot_ok, 1)
                nc.vector.tensor_tensor(masked[:, :, 0:V], uf[:, :, 0:V], bcast(mask_f[:], V), ALU.mult).then_inc(masked_ok, 1)
                dve.wait_ge(in_tab, 16 * 7)
                dve.wait_ge(pp_ready, 1)
                for c in range(KC):
                    nc.vector.tensor_copy(lhs_t[:, KC + c, 0:V], proj_bT[:, c:c + 1].to_broadcast([P, V])).then_inc(lhs_ok, 1)
                    nc.vector.tensor_copy(lhs_t[:, KC + c, V:2 * V], psum[7][:, c * V:(c + 1) * V]).then_inc(lhs_ok, 1)
                dve.wait_ge(cnt_ready, 1)
                for n in range(2):
                    nc.vector.tensor_scalar(cnt_len[:, 16 * n:16 * n + 16].rearrange("p (b o) -> p b o", o=1),
                                            cnt_ps[n][:, :, V:V + 1], 1.0, None, ALU.max).then_inc(len_ok, 1)
                dve.wait_ge(len_ok, 2)
                nc.vector.reciprocal(share[:], cnt_len[:]).then_inc(len_ok, 1)
                dve.wait_ge(len_ok, 3)
                for n in range(2):
                    nc.vector.tensor_tensor(uf[:, 16 * n:16 * n + 16, V:2 * V], cnt_ps[n][:, :, 0:V],
                                            share[:, 16 * n:16 * n + 16].rearrange("p (b o) -> p b o", o=1)
                                            .to_broadcast([P, 16, V]), ALU.mult).then_inc(shares_ok, 1)
                dve.wait_ge(tab_ready, 1)
                dve.wait_ge(zeroed, 3)
                tab = psum[6][0:2 * V, 0:D]
                nc.vector.reduce_sum(msum[0:2 * V, 0:1], tab, AX.X).then_inc(tab_step, 1)
                dve.wait_ge(tab_step, 1)
                nc.vector.tensor_scalar(msum[0:2 * V, 1:2], msum[0:2 * V, 0:1], -1.0 / D, None, ALU.mult).then_inc(tab_step, 1)
                dve.wait_ge(tab_step, 2)
                nc.vector.tensor_scalar(tt[0:2 * V, 0, :], tab, msum[0:2 * V, 1:2], None, ALU.add).then_inc(tab_step, 1)
                dve.wait_ge(tab_step, 3)
                dve.wait_ge(in_row, 48)
                nc.vector.tensor_tensor(tt[0:2 * V, 1, :], tt[0:2 * V, 0, :], g_b[0:2 * V, :], ALU.mult).then_inc(tab_step, 1)
                dve.wait_ge(tts_ok, 1)
                nc.vector.scalar_tensor_tensor(out=both(tts[UD:P]), in0=both(tt[:]), scalar=T_SCALE, in1=both(tts[0:UD]),
                                               op0=ALU.mult, op1=ALU.subtract).then_inc(tts_ok, 1)
                dve.wait_ge(in_lnb, 16)
                nc.vector.tensor_copy(mb[0:2 * V, :], tt[0:2 * V, 1, :]).then_inc(tab_step, 1)
                dve.wait_ge(tab_step, 5)
                nc.vector.reduce_sum(msum[:, 2:3], mb[:], AX.X).then_inc(tab_step, 1)
                dve.wait_ge(tab_step, 6)
                nc.vector.tensor_scalar(msum[:, 3:4], msum[:, 2:3], -1.0 / D, None, ALU.mult).then_inc(tab_step, 1)
                dve.wait_ge(tab_step, 7)
                nc.vector.tensor_scalar(mbo[:], mb[:], msum[:, 3:4], None, ALU.add).then_inc(m_ok, 1)

                def lo_part(g, hi_sem, out_sem):
                    dve.wait_ge(hi_sem, g.val(1, 1))
                    nc.vector.tensor_tensor(ub_g[:, g.val(), :, 1, :],
                                            psum[2 + g.par][:].rearrange("p (f t) -> p f t", f=GB),
                                            ub_g[:, g.val(), :, 0, :], ALU.subtract).then_inc(out_sem, 1)

                with dve.Fori(0, NG // 2) as k:
                    for g in range(2):
                        lo_part(At(k, g), hi_a, lo_a)
                dve.wait_ge(mt_ready, 1)
                nc.vector.tensor_copy(both(mt[:]), psum[7][:, 0:KC * UD]).then_inc(mt_ok, 1)
                dve.wait_ge(mhi_ok, 1)
                nc.vector.scalar_tensor_tensor(out=mr[UD:P, :], in0=mbo[:], scalar=Y_SCALE, in1=mr[0:UD, :],
                                               op0=ALU.mult, op1=ALU.subtract).then_inc(mhi_ok, 1)
                dve.wait_ge(in_qk_b, 48)
                for n in range(3):
                    dve.wait_ge(qkv_ready, n + 1)
                    src = psum[4 + n][:].rearrange("p (c u) -> p c u", c=HD)
                    nc.vector.tensor_copy(qkv_t[:, n], src).then_inc(qkv_ok, 1)
                    dve.wait_ge(qkv_ok, 2 * n + 1)
                    nc.vector.tensor_copy(qkv_t[:, n, :, ONE:ONE + 1], bT[:, n, :].rearrange("p (c o) -> p c o", o=1))\
                        .then_inc(qkv_ok, 1)
                dve.wait_ge(ghi_ok, len(G_PARTS))
                for hf, ab, m in G_PARTS:
                    nc.vector.scalar_tensor_tensor(out=gp[UD:P, hf, m::2, ab, :], in0=g_part(hf, ab, m),
                                                   scalar=G_SCALE * K ** -0.5, in1=gp[0:UD, hf, m::2, ab, :],
                                                   op0=ALU.mult, op1=ALU.subtract).then_inc(glo_ok, 1)
                for n in range(4):
                    dve.wait_ge(z_ready, n + 1)
                    nc.vector.tensor_scalar(z[:, Z_BANKS[n][0]:Z_BANKS[n][1] + 1:2, :],
                                            psum[4 + n % 3][:].rearrange("p (a n) -> p a n", a=2),
                                            Y_SCALE, None, ALU.mult).then_inc(z_ok, 1)
                dve.wait_ge(in_w12, 48)
                dve.wait_ge(in_b2, 16 * 8)
                dve.wait_ge(zeroed, 8)
                parts = ((both(w1s[:, 0]), both(w1s[:, 1]), stage2[:, 0, :]), (both(w2s[:, 0]), both(w2s[:, 1]), stage2[:, 1, :]),
                         (both(wgs[:, 0]), both(wgs[:, 1]), both(wg_f[:])))
                for n, (hi, lo, src) in enumerate(parts):
                    nc.vector.tensor_scalar(hi, src, W_SCALE, None, ALU.mult).then_inc(w_hi, 1)
                for r in (32, 64):
                    nc.vector.tensor_scalar(b2s[r:r + E, :], b2_f[r:r + E, :], W_SCALE, None, ALU.mult).then_inc(w_hi, 1)
                for n, (hi, lo, src) in enumerate(parts):
                    dve.wait_ge(w_hi, n + 1)
                    nc.vector.scalar_tensor_tensor(out=lo, in0=src, scalar=W_SCALE, in1=hi, op0=ALU.mult,
                                                   op1=ALU.subtract).then_inc(w_hi, 1)
                dve.wait_ge(w_hi, 5)
                nc.vector.scalar_tensor_tensor(out=b2s[64:64 + E, :], in0=b2_f[64:64 + E, :], scalar=W_SCALE,
                                               in1=b2s[64:64 + E, :], op0=ALU.mult, op1=ALU.subtract).then_inc(w_hi, 1)
                dve.wait_ge(r1_ok, 1)

                def h_of(b):
                    dve.wait_ge(f_b, b.val(1, 1))
                    if b.from_(2):
                        dve.wait_ge(tok_b, b.val(1, -1))
                    nc.vector.scalar_tensor_tensor(out=ht[:, b.par, :], in0=psum[4 + b.off % 4][:, 0:D],
                                                   scalar=r1[:, bass.ds(b.val(), 1)], in1=b_b[:],
                                                   op0=ALU.mult, op1=ALU.add).then_inc(h_b, 1)

                def stats_of(b):
                    dve.wait_ge(h_b, b.val(1, 1))
                    nc.vector.bn_stats(bst[:, b.par, :], ht[:, b.par, :]).then_inc(bn_b, 1)
                    dve.wait_ge(met, 1)
                    dve.wait_ge(bn_b, b.val(1, 1))
                    nc.vector.bn_aggr(mvh[:, b.par, :], bst[:, b.par, :]).then_inc(ag_b, 1)
                    dve.wait_ge(ag_b, b.val(1, 1))
                    nc.vector.tensor_copy(vh[:, bass.ds(b.val(), 1)], mvh[:, b.par, 1:2]).then_inc(mv_b, 1)

                for b in range(GB):
                    h_of(At(0, b))
                    stats_of(At(0, b))
                with dve.Fori(0, NG - 1) as k:
                    for b in range(GB, 2 * GB):
                        h_of(At(k * 2, b))
                        stats_of(At(k * 2, b))
                dve.wait_ge(r2_ok, 1)
                nc.vector.tensor_tensor(r12[:], r1[:], r2[:], ALU.mult).then_inc(r12_ok, 1)
                dve.wait_ge(r12_ok, 1)
                dve.wait_ge(st_a, 2 * NG)
                nc.vector.scalar_tensor_tensor(out=uf[:, :, 0:2 * V], in0=uf[:, :, 0:2 * V], scalar=T_SCALE,
                                               in1=bcast(r12[:], 2 * V), op0=ALU.mult, op1=ALU.mult).then_inc(u_ok, 1)
                nc.vector.tensor_copy(uf[:, :, R2:R2 + 1], r2[:].rearrange("p (b o) -> p b o", o=1)).then_inc(u_ok, 1)
                nc.vector.memset(uf[:, :, ONE:SHIFT + 1], 1.0).then_inc(u_ok, 1)
                with dve.Fori(0, NG // 2) as k:
                    for g in range(2):
                        lo_part(At(k, g), hi_c, lo_c)

            @block.tensor
            def _(pe):
                pe.wait_ge(in_tab, 16 * 7)
                for c in range(KC):
                    mm = nc.tensor.matmul(psum[7][:, c * V:(c + 1) * V], proj_w[:, c * P:(c + 1) * P], pcaT[:],
                                          start=True, stop=True)
                mm.then_inc(pp_ready, 1)
                pe.wait_ge(masked_ok, 2)
                for n in range(2):
                    mm = nc.tensor.matmul(psum[n][:, 0:16 * (V + 1)], band[:],
                                          masked[:, 16 * n:16 * n + 16, :].rearrange("p b v -> p (b v)"), start=True, stop=True)
                mm.then_inc(cnt_ready, 1)
                pe.wait_ge(lhs_ok, 2 * KC)
                pe.wait_ge(zeroed, 9)
                for c in range(2 * KC):
                    nc.tensor.matmul(psum[6][0:UD, 0:D], lhs_t[:, c, :], fus_w[:, c, :], start=(c == 0), stop=False)
                nc.tensor.matmul(psum[6][0:UD, 0:D], row1[:], fus_b[:], start=False, stop=True).then_inc(tab_ready, 1)

                def transposes(g, staged, hi_sem, lo_sem, done):
                    pe.wait_ge(staged, g.val(2, 2))
                    if g.from_(2):
                        pe.wait_ge(lo_sem, g.val(1, -1))
                    for f in range(GB):
                        tp = nc.tensor.transpose(psum[2 + g.par][:, f * P:(f + 1) * P],
                                                 stg[:, g.par, f, :, :].rearrange("p c u -> p (c u)"), ident[:])
                    tp.then_inc(done, 1)

                def table_rows(b, bank, col, done):
                    for part in range(2):
                        mm = nc.tensor.matmul(psum[bank][:, 0:D], ub[:, b.val(), part, :], tts[:, col, :],
                                              start=(part == 0), stop=(part == 1))
                    mm.then_inc(done, 1)

                def group_a(g):
                    transposes(g, st_a, hi_a, lo_a, t_a)

                def group_f(g, gb):
                    pe.wait_ge(lo_a, g.val(1, 1))
                    for f in range(GB):
                        b = At(gb, (g.off * GB) + f)
                        if g.from_(1):
                            pe.wait_ge(sq_a, b.val(1, 1 - GB))
                        table_rows(b, 4 + f, 0, f_a)

                pe.wait_ge(tts_ok, 2)
                group_a(At(0, 0))
                group_a(At(0, 1))
                group_f(At(0, 0), 0)
                group_f(At(0, 1), 0)
                with pe.Fori(0, NG // 2 - 1) as k:
                    group_a(At(k, 2))
                    group_a(At(k, 3))
                    group_f(At(k, 2), k * GB)
                    group_f(At(k, 3), k * GB)
                pe.wait_ge(in_bo, 16)
                pe.wait_ge(sq_a, B)
                for c in range(KC):
                    tp = nc.tensor.transpose(psum[7][:, c * UD:(c + 1) * UD], mbo[:, c * P:(c + 1) * P], ident[0:UD, 0:UD])
                tp.then_inc(mt_ready, 1)
                pe.wait_ge(mt_ok, 1)
                pe.wait_ge(in_qkv, 48)
                for n in range(3):
                    for c in range(HD):
                        for kc in range(KC):
                            mm = nc.tensor.matmul(psum[4 + n][:, c * UD:(c + 1) * UD], stage_w[:, n, kc, c * P:(c + 1) * P],
                                                  mt[:, kc, :], start=(kc == 0), stop=(kc == KC - 1))
                    mm.then_inc(qkv_ready, 1)
                pe.wait_ge(qkv_ok, 6)
                for h in range(H):
                    k0 = K * (h % 2)
                    mm = nc.tensor.matmul(psum[h % 2][0:UD, (h // 2) * UD:(h // 2 + 1) * UD], qkv_t[k0:k0 + K, 0, h // 2, :],
                                          qkv_t[k0:k0 + K, 1, h // 2, :], start=True, stop=True)
                    if h >= H - 2:
                        mm.then_inc(g_ready, 1)
                pe.wait_ge(in_wo, 16)
                for n, chunks in enumerate(Z_BANKS):
                    if n >= 3:
                        pe.wait_ge(z_ok, n - 2)
                    for m, p in enumerate(chunks):
                        for ab in range(2):
                            h = 8 * (p // 4) + 4 * ab + p % 4
                            k0 = K * (h % 2)
                            mm = nc.tensor.matmul(psum[4 + n % 3][ab * UD:(ab + 1) * UD, m * D:(m + 1) * D],
                                                  qkv_t[k0:k0 + K, 2, h // 2, :], wo_v[k0:k0 + K, h // 2, :],
                                                  start=True, stop=True)
                    mm.then_inc(z_ready, 1)
                pe.wait_ge(z_ok, 4)
                for b in range(GB):
                    table_rows(At(0, b), 4 + b, 1, f_b)
                with pe.Fori(0, NG - 1) as k:
                    for b in range(GB):
                        i = At(k * 2, GB + b)
                        pe.wait_ge(h_b, i.val(1, 1 - GB))
                        table_rows(i, 4 + b, 1, f_b)
                for g in range(2):
                    transposes(At(0, g), st_c, hi_c, lo_c, t_c)
                with pe.Fori(0, NG // 2 - 1) as k:
                    for g in range(2, 4):
                        transposes(At(k, g), st_c, hi_c, lo_c, t_c)

        one.close()

        xt_all = sb("xt_all", [P, B, 2, KC, P], F16)
        two = ctx.enter_context(ExitStack())

        def sb2(name, shape, dt=F32):
            return sb(name, shape, dt, two)

        ua = sb2("ua", [P, 2, 2, P], F16)
        uy = sb2("uy", [P, 2, 2, P], F16)
        uc = sb2("uc", [P, 2, UD])
        qs = sb2("qs", [P, 2, H, P], F16)
        probs = sb2("probs", [P, 2, H, P])
        mx = sb2("mx", [P, 2, H])
        mrow = sb2("mrow", [H, 2, P], F16)
        rsum = sb2("rsum", [P, 2, 8])
        cn = sb2("cn", [P, 2, 4, P])
        ctx_t = sb2("ctx_t", [P, 2, HD, P])
        bsy, mvy = sb2("bsy", [P, 2, 6]), sb2("mvy", [P, 2, 2])
        vy, ry = sb2("vy", [P, 2]), sb2("ry", [P, 2])
        ytmp = sb2("ytmp", [P, D])
        bsx, mvc = sb2("bsx", [P, 6]), sb2("mvc", [P, 2, 2])
        vx, rx = sb2("vx", [P, 2]), sb2("rx", [P, 2])
        xc = sb2("xc", [P, 2, D])
        xtc = sb2("xtc", [P, 2, 2, KC, P], F16)

        QP, SM, ST, CB, MISC, YB = psum[0], psum[1], psum[2:4], psum[4:6], psum[6], psum[7]

        ua_in = [sem(f"ua_in{n}") for n in range(2)]
        uy_in = [sem(f"uy_in{n}") for n in range(2)]
        shift_in = [sem(f"shift_in{n}") for n in range(2)]
        xt_out = [sem(f"xt_out{n}") for n in range(2)]
        q_ready, sm_ready, st_ready, mt2_ready, pv_ready, y_ready, xt_ready, lg_ready = (
            sem(n) for n in ("q_ready", "sm_ready", "st_ready", "mt2_ready", "pv_ready", "y_ready", "xt_ready", "lg_ready"))
        cn_done, t_ready = sem("cn_done"), sem("t_ready")
        qhi_done, exp_done, mrow_done, xhi_done = sem("qhi_done"), sem("exp_done"), sem("mrow_done"), sem("xhi_done")
        qlo_done, max_done, rs_done, c_done, bsy_done, ystat, y_read, h2_done, bsx_done, ag_done, xstat, x_done, xlo_done, \
            lg_done = (sem(n) for n in ("qlo_done", "max_done", "rs_done", "c_done", "bsy_done", "ystat", "y_read", "h2_done",
                                        "bsx_done", "ag_done", "xstat", "x_done", "xlo_done", "lg_done"))
        vy_done, ry_done, vx_done, rx_done = sem("vy_done"), sem("ry_done"), sem("vx_done"), sem("rx_done")

        def steps(eng, step):
            def at(n):
                step(At(0, n), *(0 <= n + m < B for m in (2, 1, 0, -1, -2, -3)))

            for n in range(-2, 5):
                at(n)
            with eng.Fori(0, B // 2 - 4) as k:
                for off in (5, 6):
                    step(At(k, off), True, True, True, True, True, True)
            for n in range(B - 3, B + 3):
                at(n)

        with nc.Block() as block:
            @block.sync
            def _(sp):
                def load_ua(b):
                    if b.from_(2):
                        sp.wait_ge(st_ready, b.val(4, -4))
                    sp.dma_start(both(ua[:, b.par]), ub[:, b.val()].rearrange("p a t -> p (a t)")).then_inc(ua_in[b.par], 16)

                def load_uy(b):
                    if b.from_(2):
                        sp.wait_ge(y_ready, b.val(1, -1))
                    sp.dma_start(both(uy[:, b.par]), ub[:, b.val()].rearrange("p a t -> p (a t)")).then_inc(uy_in[b.par], 16)
                    sp.dma_start(uc[:, b.par], uf[:, b.val()]).then_inc(uy_in[b.par], 16)

                def step(i, q2, nxt, now, outp, res, xs):
                    if xs:
                        b = i.plus(-3)
                        sp.wait_ge(xlo_done, b.val(1, 1))
                        sp.dma_start(xt_all[:, b.val()].rearrange("p a c t -> p (a c t)"),
                                     xtc[:, b.par].rearrange("p a c t -> p (a c t)")).then_inc(xt_out[b.par], 16)
                    if now:
                        load_uy(i)
                    if nxt:
                        b = i.plus(1)
                        sp.wait_ge(mrow_done, b.val(1, 1))
                        sp.dma_start(qs[SHIFT:SHIFT + 1, b.par], mrow[:, b.par, :]).then_inc(shift_in[b.par], 16)
                    if q2:
                        load_ua(i.plus(2))

                steps(sp, step)
                for n in range(2):
                    sp.wait_ge(xt_out[n], 16 * B // 2)

            @block.gpsimd
            def _(pool):
                def root(mv, par, v, r, v_done, r_done, b, eps):
                    nc.gpsimd.tensor_tensor(v[:, par:par + 1], mv[:, par, 1:2], eps[:], ALU.add).then_inc(v_done, 1)
                    pool.wait_ge(v_done, b.val(1, 1))
                    nc.gpsimd.tensor_tensor(r[:, par:par + 1], v[:, par:par + 1], mhalf[:, 0:1], ALU.pow).then_inc(r_done, 1)

                def step(i, q2, nxt, now, outp, res, xs):
                    if res:
                        b = i.plus(-2)
                        pool.wait_ge(ystat, b.val(1, 1))
                        root(mvy, b.par, vy, ry, vy_done, ry_done, b, eps_y)
                        pool.wait_ge(ag_done, b.val(1, 1))
                        root(mvc, b.par, vx, rx, vx_done, rx_done, b, eps_x)

                steps(pool, step)

            @block.scalar
            def _(act):
                nc.scalar.preload_act_table(ACT.Exp)

                def q_hi(b, hf):
                    act.wait_ge(q_ready, b.val(2, hf + 1))
                    if b.from_(2):
                        act.wait_ge(st_ready, b.val(4, -4))
                    for ab in range(2):
                        r = slice(ab * UD, ab * UD + UD)
                        last = nc.scalar.activation(both(qs[r, b.par, 8 * hf + 4 * ab:8 * hf + 4 * ab + 4, :]), QP[r, :],
                                                    ACT.Copy, scale=1.0 / G_SCALE)
                    last.then_inc(qhi_done, 1)

                def exps(b, j):
                    act.wait_ge(st_ready, b.val(4, j + 1))
                    if b.from_(2):
                        act.wait_ge(pv_ready, b.val(2, j // 2 - 3))
                    nc.scalar.activation(both(probs[:, b.par, 4 * j:4 * j + 4, :]), ST[j % 2][:], ACT.Exp).then_inc(exp_done, 1)

                def context_t(b, hf):
                    act.wait_ge(t_ready, b.val(2, hf + 1))
                    if b.from_(2):
                        act.wait_ge(y_ready, b.val(1, -1))
                    nc.scalar.activation(both(ctx_t[:, b.par, 4 * hf:4 * hf + 4, :]), CB[hf][:], ACT.Copy).then_inc(c_done, 1)

                def step(i, q2, nxt, now, outp, res, xs):
                    if now:
                        exps(i, 0)
                        exps(i, 1)
                    if xs:
                        b = i.plus(-3)
                        act.wait_ge(xt_ready, b.val(1, 1))
                        if b.from_(2):
                            act.wait_ge(xt_out[b.par], b.half(16))
                            act.wait_ge(lg_ready, b.val(1, -1))
                        nc.scalar.activation(xtc[:, b.par, 0].rearrange("p c t -> p (c t)"), MISC[:, 0:D], ACT.Copy)\
                            .then_inc(xhi_done, 1)
                    if now:
                        exps(i, 2)
                    if outp:
                        context_t(i.plus(-1), 0)
                    if now:
                        exps(i, 3)
                    if outp:
                        context_t(i.plus(-1), 1)
                    if nxt:
                        b = i.plus(1)
                        act.wait_ge(mt2_ready, b.val(1, 1))
                        if b.from_(2):
                            act.wait_ge(shift_in[b.par], b.half(16))
                        nc.scalar.activation(mrow[:, b.par, :], MISC[0:H, 0:P], ACT.Copy, scale=-1.0).then_inc(mrow_done, 1)
                    if q2:
                        q_hi(i.plus(2), 0)
                        q_hi(i.plus(2), 1)

                steps(act, step)

            @block.vector
            def _(dve):
                def q_lo(b, hf):
                    dve.wait_ge(qhi_done, b.val(2, hf + 1))
                    for ab in range(2):
                        r, o = slice(ab * UD, ab * UD + UD), slice((1 - ab) * UD, (1 - ab) * UD + UD)
                        heads = slice(8 * hf + 4 * ab, 8 * hf + 4 * ab + 4)
                        last = nc.vector.scalar_tensor_tensor(out=both(qs[o, b.par, heads, :]), in0=QP[r, :],
                                                              scalar=1.0 / G_SCALE, in1=both(qs[r, b.par, heads, :]),
                                                              op0=ALU.mult, op1=ALU.subtract)
                    last.then_inc(qlo_done, 1)

                def maxima(b, j):
                    dve.wait_ge(sm_ready, b.val(4, j + 1))
                    if b.from_(2):
                        dve.wait_ge(mt2_ready, b.val(1, -1))
                    nc.vector.tensor_reduce(mx[:, b.par, 4 * j:4 * j + 4], SM[:].rearrange("p (h k) -> p h k", h=4), AX.X,
                                            ALU.max).then_inc(max_done, 1)

                def context(b, hf):
                    dve.wait_ge(pv_ready, b.val(2, hf + 1))
                    c = CB[hf][:].rearrange("p (h u) -> p h u", u=UD)
                    r = rsum[:, hf].rearrange("p (h o) -> p h o", o=1)
                    nc.vector.reciprocal(r, c[:, :, ONE:ONE + 1]).then_inc(rs_done, 1)
                    dve.wait_ge(rs_done, b.val(2, hf + 1))
                    nc.vector.tensor_tensor(cn[:, hf].rearrange("p t (a u) -> p (t a) u", u=UD), c,
                                            r.to_broadcast([P, 8, UD]), ALU.mult).then_inc(cn_done, 1)

                def output_stats(b):
                    dve.wait_ge(y_ready, b.val(1, 1))
                    nc.vector.bn_stats(bsy[:, b.par, :], YB[:, 0:D]).then_inc(bsy_done, 1)
                    dve.wait_ge(met, 1)
                    dve.wait_ge(bsy_done, b.val(1, 1))
                    nc.vector.bn_aggr(mvy[:, b.par, :], bsy[:, b.par, :]).then_inc(ystat, 1)

                def x_lo(b):
                    dve.wait_ge(xhi_done, b.val(1, 1))
                    nc.vector.tensor_tensor(xtc[:, b.par, 1].rearrange("p c t -> p (c t)"), MISC[:, 0:D],
                                            xtc[:, b.par, 0].rearrange("p c t -> p (c t)"), ALU.subtract)\
                        .then_inc(xlo_done, 1)

                def h2(b):
                    dve.wait_ge(ystat, b.val(1, 1))
                    nc.vector.scalar_tensor_tensor(out=ytmp[:], in0=YB[:, 0:D], scalar=mvy[:, b.par, 0:1], in1=ga1_b[:],
                                                   op0=ALU.subtract, op1=ALU.mult).then_inc(y_read, 1)
                    dve.wait_ge(y_read, b.val(1, 1))
                    dve.wait_ge(ry_done, b.val(1, 1))
                    nc.vector.scalar_tensor_tensor(out=tok[:, b.val(), :], in0=ytmp[:], scalar=ry[:, b.par:b.par + 1],
                                                   in1=tok[:, b.val(), :], op0=ALU.mult, op1=ALU.add).then_inc(h2_done, 1)
                    dve.wait_ge(met, 1)
                    dve.wait_ge(h2_done, b.val(1, 1))
                    nc.vector.bn_stats(bsx[:], tok[:, b.val(), :]).then_inc(bsx_done, 1)
                    dve.wait_ge(met, 1)
                    dve.wait_ge(bsx_done, b.val(1, 1))
                    nc.vector.bn_aggr(mvc[:, b.par, :], bsx[:]).then_inc(ag_done, 1)

                def x_rows(b):
                    dve.wait_ge(ag_done, b.val(1, 1))
                    nc.vector.tensor_copy(mvx[:, b.val(), :], mvc[:, b.par, :]).then_inc(xstat, 1)
                    dve.wait_ge(rx_done, b.val(1, 1))
                    if b.from_(2):
                        dve.wait_ge(xt_ready, b.val(1, -1))
                    nc.vector.tensor_scalar(xc[:, b.par, :], tok[:, b.val(), :], mvc[:, b.par, 0:1],
                                            rx[:, b.par:b.par + 1], ALU.subtract, ALU.mult).then_inc(x_done, 1)

                def step(i, q2, nxt, now, outp, res, xs):
                    if nxt:
                        q_lo(i.plus(1), 1)
                        maxima(i.plus(1), 0)
                    if res:
                        output_stats(i.plus(-2))
                    if outp:
                        context(i.plus(-1), 0)
                    if nxt:
                        maxima(i.plus(1), 1)
                    if xs:
                        x_lo(i.plus(-3))
                    if outp:
                        context(i.plus(-1), 1)
                    if nxt:
                        maxima(i.plus(1), 2)
                    if res:
                        h2(i.plus(-2))
                    if nxt:
                        maxima(i.plus(1), 3)
                    if xs:
                        b = i.plus(-3)
                        dve.wait_ge(lg_ready, b.val(1, 1))
                        nc.vector.tensor_scalar(lg[:, b.val(), :], YB[:, D:D + E], 1.0 / W_SCALE, None, ALU.mult)\
                            .then_inc(lg_done, 1)
                    if res:
                        x_rows(i.plus(-2))
                    if q2:
                        q_lo(i.plus(2), 0)

                steps(dve, step)

            @block.tensor
            def _(pe):
                def q_rows(b, hf):
                    if hf == 0:
                        pe.wait_ge(ua_in[b.par], b.half(16, 16))
                    if b.from_(1) or hf:
                        pe.wait_ge(qlo_done, b.val(2, hf))
                    for t in range(4):
                        for part in range(2):
                            mm = nc.tensor.matmul(QP[:, t * P:(t + 1) * P], gp[:, hf, t].rearrange("p a u -> p (a u)"),
                                                  ua[:, b.par, part, :], start=(part == 0), stop=(part == 1))
                    mm.then_inc(q_ready, 1)

                def score_rows(b, j):
                    if j % 2 == 0:
                        pe.wait_ge(qlo_done, b.val(2, j // 2 + 1))
                    if b.from_(1) or j:
                        pe.wait_ge(max_done, b.val(4, j))
                    for t in range(4):
                        mm = nc.tensor.matmul(SM[:, t * P:(t + 1) * P], qs[:, b.par, 4 * j + t, :], ua[:, b.par, 0, :],
                                              start=True, stop=True)
                    mm.then_inc(sm_ready, 1)

                def score_cols(b, j):
                    if j == 0:
                        pe.wait_ge(shift_in[b.par], b.half(16, 16))
                    if b.from_(1) or j >= 2:
                        pe.wait_ge(exp_done, b.val(4, j - 1))
                    for part in range(2):
                        mm = nc.tensor.matmul(ST[j % 2][:], ua[:, b.par, part, :], both(qs[:, b.par, 4 * j:4 * j + 4, :]),
                                              start=(part == 0), stop=(part == 1))
                    mm.then_inc(st_ready, 1)

                def values(b, hf):
                    if hf == 0:
                        pe.wait_ge(uy_in[b.par], b.half(32, 32))
                    pe.wait_ge(exp_done, b.val(4, 2 * hf + 2))
                    if b.from_(1):
                        pe.wait_ge(c_done, b.val(2, hf - 1))
                    for t in range(4):
                        for ab in range(2):
                            c = (2 * t + ab) * UD
                            mm = nc.tensor.matmul(CB[hf][:, c:c + UD], probs[:, b.par, 8 * hf + 4 * ab + t, :], uc[:, b.par, :],
                                                  start=True, stop=True)
                    mm.then_inc(pv_ready, 1)

                def turn(b, hf):
                    pe.wait_ge(cn_done, b.val(2, hf + 1))
                    for t in range(4):
                        tp = nc.tensor.transpose(CB[hf][:, t * P:(t + 1) * P], cn[:, hf, t, :], ident[:])
                    tp.then_inc(t_ready, 1)

                def output(b, chunks):
                    for p in chunks:
                        if p % 4 == 0:
                            pe.wait_ge(c_done, b.val(2, p // 4 + 1))
                        nc.tensor.matmul(YB[:, 0:D], ctx_t[:, b.par, p, :], z[:, p, :], start=(p == 0), stop=False)

                def residual(b):
                    for part in range(2):
                        mm = nc.tensor.matmul(YB[:, 0:D], uy[:, b.par, part, :], mr[:], start=False, stop=(part == 1))
                    mm.then_inc(y_ready, 1)

                def x_cols(b):
                    pe.wait_ge(x_done, b.val(1, 1))
                    if isinstance(b.pair, int) and b.off + 3 >= B:
                        pe.wait_ge(mrow_done, B)
                        if b.off + 3 > B:
                            pe.wait_ge(xlo_done, b.val())
                    else:
                        pe.wait_ge(mrow_done, b.val(1, 4))
                    for c in range(KC):
                        tp = nc.tensor.transpose(MISC[:, c * P:(c + 1) * P], xc[:, b.par, c * P:(c + 1) * P], ident[:])
                    tp.then_inc(xt_ready, 1)

                def logits(b):
                    pe.wait_ge(xlo_done, b.val(1, 1))
                    if isinstance(b.pair, int) and b.off + 1 >= B:
                        pe.wait_ge(y_read, B)
                        pe.wait_ge(lg_done, b.val())
                    else:
                        pe.wait_ge(y_read, b.val(1, 2))
                    n = 0
                    for c in range(KC):
                        for xp, wp in ((0, 0), (0, 1), (1, 0)):
                            mm = nc.tensor.matmul(YB[:, D:D + E], xtc[:, b.par, xp, c, :], wgs[:, wp, c, :],
                                                  start=(n == 0), stop=(n == 5))
                            n += 1
                    mm.then_inc(lg_ready, 1)

                def maxima_cols(b):
                    pe.wait_ge(max_done, b.val(4, 4))
                    if b.from_(4):
                        pe.wait_ge(xlo_done, b.val(1, -3))
                    nc.tensor.transpose(MISC[0:H, 0:P], mx[:, b.par, :], ident[:]).then_inc(mt2_ready, 1)

                def step(i, q2, nxt, now, outp, res, xs):
                    for j in range(4):
                        if nxt:
                            score_rows(i.plus(1), j)
                        if now:
                            score_cols(i, j)
                        if outp:
                            (values if j < 2 else turn)(i.plus(-1), j % 2)
                        if xs and j == 0:
                            x_cols(i.plus(-3))
                        if xs and j == 2:
                            logits(i.plus(-3))
                    if nxt:
                        maxima_cols(i.plus(1))
                    if outp:
                        b = i.plus(-1)
                        if b.from_(1):
                            pe.wait_ge(y_read, b.val())
                        if b.from_(2):
                            pe.wait_ge(lg_done, b.val(1, -1))
                        output(b, range(0, 4))
                    if q2:
                        q_rows(i.plus(2), 0)
                    if outp:
                        output(b, range(4, 6))
                    if q2:
                        q_rows(i.plus(2), 1)
                    if outp:
                        output(b, range(6, 8))
                        residual(b)

                steps(pe, step)

        two.close()

        b2_rows = (32, 64)
        takes = sb("takes", [P, B, S], F16)
        three = ctx.enter_context(ExitStack())

        def sb3(name, shape, dt=F32):
            return sb(name, shape, dt, three)

        countdown = sb3("countdown", [P, E])
        gl, ge, gs, gw, gp1, gs2, gp2, gr = (sb3(n, [P, B, E]) for n in ("gl", "ge", "gs", "gw", "gp1", "gs2", "gp2", "gr"))
        gm = sb3("gm", [P, 8, B])
        den, rden = sb3("den", [P, E]), sb3("rden", [P, E])
        NT = B * E // P
        rt = sb3("rt", [P, NT, S])
        best = sb3("best", [P, NT, 8])
        chosen, unchosen = sb3("chosen", [P, NT, S], F16), sb3("unchosen", [P, NT, S], F16)

        gate_steps = []
        in_cd, gate, g_exp, rt_ready, rt_ok, best_ok, repl_ok, chosen_ok, takes_zero, takes_in, takes_in2 = (
            sem(n) for n in ("in_cd", "gate", "g_exp", "rt_ready", "rt_ok", "best_ok", "repl_ok", "chosen_ok",
                             "takes_zero", "takes_in", "takes_in2"))

        def per_seq(t):
            return t.rearrange("p (b o) -> p b o", o=1).to_broadcast([P, B, E])

        def per_expert(t):
            return t.rearrange("p (o e) -> p o e", o=1).to_broadcast([P, B, E])

        with nc.Block() as block:
            @block.sync
            def _(sp):
                sp.dma_start(countdown[:], d["countdown"]).then_inc(in_cd, 16)
                sp.wait_ge(chosen_ok, 2)
                sp.wait_ge(takes_zero, 1)
                for n in range(P // E):
                    rows = slice(n * E, (n + 1) * E)
                    sp.dma_start(takes[0:E, n::P // E, :], unchosen[rows]).then_inc(takes_in, 16)
                    sp.dma_start(takes[b2_rows[0]:b2_rows[0] + E, n::P // E, :], chosen[rows]).then_inc(takes_in, 16)
                sp.wait_ge(takes_in, 16 * 2 * P // E)

            @block.gpsimd
            def _(pool):
                nc.gpsimd.memset(takes[:], 0.0).then_inc(takes_zero, 1)
                pool.wait_ge(takes_zero, 1)
                pool.wait_ge(chosen_ok, 2)
                for n in range(P // E):
                    rows = slice(n * E, (n + 1) * E)
                    pool.dma_start(takes[b2_rows[1]:b2_rows[1] + E, n::P // E, :], chosen[rows]).then_inc(takes_in2, 16)
                pool.wait_ge(takes_in2, 16 * P // E)

            @block.scalar
            def _(act):
                act.wait_ge(gate, 3)
                nc.scalar.activation(both(ge[:]), both(gl[:]), ACT.Exp).then_inc(g_exp, 1)

            @block.vector
            def _(dve):
                step = [0]

                def then(ins):
                    step[0] += 1
                    ins.then_inc(gate, 1)
                    dve.wait_ge(gate, step[0])

                then(nc.vector.tensor_tensor(gl[:], lg[:], per_expert(bg_b[:]), ALU.add))
                then(nc.vector.tensor_reduce(gm[:, 0, :], gl[:], AX.X, ALU.max))
                then(nc.vector.tensor_tensor(gl[:], gl[:], per_seq(gm[:, 0, :]), ALU.subtract))
                dve.wait_ge(g_exp, 1)
                then(nc.vector.tensor_reduce(gm[:, 1, :], ge[:], AX.X, ALU.add))
                then(nc.vector.reciprocal(gm[:, 2, :], gm[:, 1, :]))
                then(nc.vector.tensor_tensor(gs[:], ge[:], per_seq(gm[:, 2, :]), ALU.mult))
                dve.wait_ge(in_cd, 16)

                def first_best(src, pick, m, w):
                    then(nc.vector.tensor_reduce(gm[:, m, :], src, AX.X, ALU.max))
                    then(nc.vector.tensor_tensor(gw[:], src, per_seq(gm[:, m, :]), ALU.is_equal))
                    then(nc.vector.tensor_tensor(gw[:], gw[:], per_expert(countdown[:]), ALU.mult))
                    then(nc.vector.tensor_reduce(gm[:, w, :], gw[:], AX.X, ALU.max))
                    then(nc.vector.tensor_tensor(pick, gw[:], per_seq(gm[:, w, :]), ALU.is_equal))

                first_best(gs[:], gp1[:], 3, 4)
                then(nc.vector.scalar_tensor_tensor(out=both(gs2[:]), in0=both(gp1[:]), scalar=-4.0, in1=both(gs[:]),
                                                    op0=ALU.mult, op1=ALU.add))
                first_best(gs2[:], gp2[:], 5, 6)
                then(nc.vector.tensor_tensor(both(gp1[:]), both(gp1[:]), both(gp2[:]), ALU.add))
                then(nc.vector.tensor_tensor(both(gs[:]), both(gs[:]), both(gp1[:]), ALU.mult))
                then(nc.vector.tensor_reduce(den[:], gs[:].rearrange("p b e -> p e b"), AX.X, ALU.add))
                then(nc.vector.tensor_scalar(den[:], den[:], 1e-6, None, ALU.add))
                then(nc.vector.reciprocal(rden[:], den[:]))
                then(nc.vector.tensor_tensor(gr[:], gs[:], per_expert(rden[:]), ALU.mult))
                then(nc.vector.tensor_scalar(both(gr[:]), both(gr[:]), float(B), None, ALU.mult))
                dve.wait_ge(rt_ready, 1)
                nc.vector.tensor_copy(both(rt[:]), psum[0][:]).then_inc(rt_ok, 1)
                for r in range(TAKE // 8):
                    for n in range(NT):
                        if r == 0:
                            dve.wait_ge(rt_ok, 1)
                        else:
                            dve.wait_ge(repl_ok, NT * (r - 1) + n + 1)
                        nc.vector.max(best[:, n, :], rt[:, n, :]).then_inc(best_ok, 1)
                    for n in range(NT):
                        dve.wait_ge(best_ok, NT * r + n + 1)
                        nc.vector.match_replace(rt[:, n, :], best[:, n, :], rt[:, n, :], -1.0).then_inc(repl_ok, 1)
                dve.wait_ge(repl_ok, NT * TAKE // 8)
                nc.vector.tensor_scalar(both(chosen[:]), both(rt[:]), -1.0, None, ALU.is_equal).then_inc(chosen_ok, 1)
                nc.vector.tensor_scalar(both(unchosen[:]), both(rt[:]), 0.0, -MASK_BIG, ALU.is_ge, ALU.mult)\
                    .then_inc(chosen_ok, 1)
                gate_steps.append(step[0])

            @block.tensor
            def _(pe):
                pe.wait_ge(gate, gate_steps[0])
                for n in range(NT):
                    tp = nc.tensor.transpose(psum[0][:, n * P:(n + 1) * P],
                                             gr[:, n * (P // E):(n + 1) * (P // E), :].rearrange("p b e -> p (b e)"), ident[:])
                tp.then_inc(rt_ready, 1)

        three.close()

        NH = 4
        xg = sb("xg", [P, 2, GB, 2, KC, P], F16)
        hid = sb("hid", [P, 2, 2, NJ, GB * S], F16)
        x64 = sb("x64", [P, 2, D])
        zt = sb("zt", [P, 2, D])
        zs = sb("zs", [P, 2, D])
        hb = sb("hb", [P, 2, D])
        ot = sb("ot", [P, 2, D])
        rx_all = sb("rx_all", [P, B])
        vx_all = sb("vx_all", [P, B])
        vcol = sb("vcol", [P, B])
        bsz, mvz = sb("bsz", [P, 2, 6]), sb("mvz", [P, 2, 2])
        vz, rz = sb("vz", [P, 2]), sb("rz", [P, 2])
        HB, ZB = psum[0:NH], psum[4:6]

        xg_in, out_st = ([sem(f"{n}{m}") for m in range(2)] for n in ("xg_in", "out_st"))
        h_ready, gelu_done, ghi_done, glo_done, z_ready4 = (
            sem(n) for n in ("h_ready", "gelu_done", "ghi_done", "glo_done", "z_ready4"))
        vcol_ok, vxa_ok, rxa_ok, rxs_ok = sem("vcol_ok"), sem("vxa_ok"), sem("rxa_ok"), sem("rxs_ok")
        x64_ok, zt_ok, bsz_ok, zstat, vz_ok, rz_ok, zs_ok, hb_ok, o_ok = (
            sem(n) for n in ("x64_ok", "zt_ok", "bsz_ok", "zstat", "vz_ok", "rz_ok", "zs_ok", "hb_ok", "o_ok"))

        def groups(eng, step):
            step(At(0, 0), True, False)
            step(At(0, 1), True, True)
            with eng.Fori(0, NG // 2 - 1) as k:
                for off in (2, 3):
                    step(At(k, off), True, True)
            step(At(0, NG), False, True)

        def tile_of(g, t):
            return At(g.pair * GB, g.off * GB + t)

        with nc.Block() as block:
            @block.sync
            def _(sp):
                def load(g):
                    if g.from_(2):
                        sp.wait_ge(h_ready, g.val(NJ, -NJ))
                    sp.dma_start(xg[:, g.par].rearrange("p f a c t -> p (f a c t)"),
                                 xt_all[:].rearrange("p (g f) a c t -> p g (f a c t)", f=GB)[:, g.val()])\
                        .then_inc(xg_in[g.par], 16)

                def store(b):
                    sp.wait_ge(o_ok, b.val(1, 1))
                    sp.dma_start(out[b.val()], ot[:, b.par, :]).then_inc(out_st[b.par], 16)

                def step(g, now, res):
                    if now and g.from_(1) and not (isinstance(g.pair, int) and g.off + 1 >= NG):
                        load(g.plus(1))
                    if res:
                        for t in range(GB):
                            store(tile_of(g.plus(-1), t))

                load(At(0, 0))
                load(At(0, 1))
                step(At(0, 1), True, True)
                with sp.Fori(0, NG // 2 - 2) as k:
                    for off in (2, 3):
                        step(At(k, off), True, True)
                for n in (NG - 2, NG - 1, NG):
                    step(At(0, n), n < NG, True)
                for n in range(2):
                    sp.wait_ge(out_st[n], 16 * B // 2)

            @block.gpsimd
            def _(pool):
                pool.wait_ge(vcol_ok, 1)
                nc.gpsimd.tensor_scalar(vx_all[:], vcol[:], 1e-5, None, ALU.add).then_inc(vxa_ok, 1)
                pool.wait_ge(vxa_ok, 1)
                nc.gpsimd.tensor_tensor(rx_all[:], vx_all[:], mhalf[:], ALU.pow).then_inc(rxa_ok, 1)

                def tile(b):
                    if b.from_(2):
                        pool.wait_ge(o_ok, b.val(1, -1))
                    nc.gpsimd.tensor_tensor(hb[:, b.par, :], tok[:, b.val(), :], be2_b[:], ALU.add).then_inc(hb_ok, 1)
                    pool.wait_ge(zstat, b.val(1, 1))
                    nc.gpsimd.tensor_tensor(vz[:, b.par:b.par + 1], mvz[:, b.par, 1:2], eps_z[:], ALU.add)\
                        .then_inc(vz_ok, 1)
                    pool.wait_ge(vz_ok, b.val(1, 1))
                    nc.gpsimd.tensor_tensor(rz[:, b.par:b.par + 1], vz[:, b.par:b.par + 1], mhalf[:, 0:1], ALU.pow)\
                        .then_inc(rz_ok, 1)

                tile(At(0, 0))
                tile(At(0, 1))
                with pool.Fori(0, B // 2 - 1) as k:
                    for off in (2, 3):
                        tile(At(k, off))

            @block.scalar
            def _(act):
                nc.scalar.preload_act_table(ACT.Gelu)

                def step(g, now, res):
                    if not now:
                        return
                    for j in range(NJ):
                        bank = HB[j % NH]
                        act.wait_ge(h_ready, g.val(NJ, j + 1))
                        nc.scalar.activation(bank[:], bank[:], ACT.Gelu, bias=b1T[:, j:j + 1], scale=1.0 / W_SCALE)\
                            .then_inc(gelu_done, 1)
                        act.wait_ge(gelu_done, g.val(NJ, j + 1))
                        if g.from_(2) and j == 0:
                            act.wait_ge(z_ready4, g.val(GB, -GB))
                        nc.scalar.activation(hid[:, g.par, 0, j, :], bank[:], ACT.Copy).then_inc(ghi_done, 1)

                groups(act, step)

            @block.vector
            def _(dve):
                nc.vector.tensor_copy(vcol[:], mvx[:, :, 1:2].rearrange("p b o -> p (b o)")).then_inc(vcol_ok, 1)
                dve.wait_ge(rxa_ok, 1)
                nc.vector.tensor_scalar(rx_all[:], rx_all[:], X_SCALE, None, ALU.mult).then_inc(rxs_ok, 1)
                dve.wait_ge(rxs_ok, 1)

                def lo(g, j):
                    bank = HB[j % NH]
                    dve.wait_ge(ghi_done, g.val(NJ, j + 1))
                    nc.vector.tensor_tensor(hid[:, g.par, 1, j, :], bank[:], hid[:, g.par, 0, j, :], ALU.subtract)\
                        .then_inc(glo_done, 1)

                def x_part(b):
                    nc.vector.tensor_scalar(x64[:, b.par, :], tok[:, b.val(), :], mvx[:, b.val(), 0:1],
                                            rx_all[:, bass.ds(b.val(), 1)], ALU.subtract, ALU.mult).then_inc(x64_ok, 1)

                def stats(b):
                    dve.wait_ge(z_ready4, b.val(1, 1))
                    dve.wait_ge(x64_ok, b.val(1, 1))
                    nc.vector.tensor_tensor(zt[:, b.par, :], ZB[b.par][:, 0:D], x64[:, b.par, :], ALU.add).then_inc(zt_ok, 1)
                    dve.wait_ge(zt_ok, b.val(1, 1))
                    nc.vector.bn_stats(bsz[:, b.par, :], zt[:, b.par, :]).then_inc(bsz_ok, 1)
                    dve.wait_ge(met, 1)
                    dve.wait_ge(bsz_ok, b.val(1, 1))
                    nc.vector.bn_aggr(mvz[:, b.par, :], bsz[:, b.par, :]).then_inc(zstat, 1)

                def finish(b):
                    dve.wait_ge(zstat, b.val(1, 1))
                    nc.vector.scalar_tensor_tensor(out=zs[:, b.par, :], in0=zt[:, b.par, :], scalar=mvz[:, b.par, 0:1],
                                                   in1=ga2_b[:], op0=ALU.subtract, op1=ALU.mult).then_inc(zs_ok, 1)
                    dve.wait_ge(zs_ok, b.val(1, 1))
                    dve.wait_ge(rz_ok, b.val(1, 1))
                    dve.wait_ge(hb_ok, b.val(1, 1))
                    if b.from_(2):
                        dve.wait_ge(out_st[b.par], b.half(16))
                    nc.vector.scalar_tensor_tensor(out=ot[:, b.par, :], in0=zs[:, b.par, :], scalar=rz[:, b.par:b.par + 1],
                                                   in1=hb[:, b.par, :], op0=ALU.mult, op1=ALU.add).then_inc(o_ok, 1)

                def step(g, now, res):
                    for j in range(NJ):
                        if now:
                            lo(g, j)
                        if res and j % 2 == 0:
                            x_part(tile_of(g.plus(-1), j // 2))
                        if res and j % 2 == 1:
                            b = tile_of(g.plus(-1), j // 2)
                            stats(b)
                            if b.from_(1):
                                finish(b.plus(-1))

                groups(dve, step)
                finish(At(0, B - 1))

            @block.tensor
            def _(pe):
                def hidden(g, j):
                    n = 0
                    if j == 0:
                        pe.wait_ge(xg_in[g.par], g.half(16, 16))
                    if g.from_(1) or j >= NH:
                        pe.wait_ge(glo_done, g.val(NJ, j + 1 - NH))
                    bank = HB[j % NH]
                    nc.tensor.matmul(bank[:], expert_of[:, j, :], takes[:].rearrange("p (g f) t -> p g (f t)", f=GB)[:, g.val()],
                                     start=True, stop=False)
                    for c in range(KC):
                        for wp, xp in ((0, 0), (0, 1), (1, 0)):
                            n += 1
                            mm = nc.tensor.matmul(bank[:], w1s[:, wp, c, j * P:(j + 1) * P], xg[:, g.par, :, xp, c, :],
                                                  start=False, stop=(n == 6))
                    mm.then_inc(h_ready, 1)

                def experts_out(b, g, t):
                    if t == 0:
                        pe.wait_ge(glo_done, g.val(NJ, NJ))
                    if b.from_(2):
                        pe.wait_ge(zt_ok, b.val(1, -1))
                    nc.tensor.matmul(ZB[b.par][:, 0:D], takes[:, b.val(), :], b2s[:], start=True, stop=False)
                    for j in range(NJ):
                        for hp, wp in ((0, 0), (0, 1), (1, 0)):
                            mm = nc.tensor.matmul(ZB[b.par][:, 0:D], hid[:, g.par, hp, j, t * P:(t + 1) * P], w2s[:, wp, j, :],
                                                  start=False, stop=(j == NJ - 1 and hp == 1))
                    mm.then_inc(z_ready4, 1)

                def step(g, now, res):
                    for j in range(NJ):
                        if now:
                            hidden(g, j)
                        if res and j % 2 == 1:
                            experts_out(tile_of(g.plus(-1), j // 2), g.plus(-1), j // 2)

                groups(pe, step)

def program(nc, aps, out):
    build(nc, aps, out)


def kernel(x, mask_BS_i1_0, L0_tok_emb, L0_tok_pca_lookup, L0_tok_proj_w, L0_tok_proj_b, L0_tok_fus_w, L0_tok_fus_b,
           L0_tok_ln_g, L0_tok_ln_b, L0_attn_Wq, L0_attn_bq, L0_attn_Wk, L0_attn_bk, L0_attn_Wv, L0_attn_bv, L0_attn_Wo,
           L0_attn_bo, L0_attn_gamma, L0_attn_beta, L0_ffn_wg, L0_ffn_bg, L0_ffn_w1, L0_ffn_b1, L0_ffn_w2, L0_ffn_b2,
           L0_ffn_gamma, L0_ffn_beta):
    import concourse.bacc as bacc
    from concourse.bass_utils import run_bass_kernel_spmd

    def lay(a):
        return np.ascontiguousarray(a)

    def chunks(a, n):
        return lay(np.asarray(a).reshape(n, P, -1).transpose(1, 0, 2))

    def column(a, n):
        return lay(np.asarray(a).reshape(n, P).T)

    def row(a):
        return lay(np.asarray(a).reshape(1, -1))

    arrays = {
        "idsT": lay(np.asarray(x).T), "maskT": lay(np.asarray(mask_BS_i1_0).T),
        "embT": chunks(np.asarray(L0_tok_emb).T, KC), "pcaT": lay(np.asarray(L0_tok_pca_lookup).T),
        "proj_w": lay(L0_tok_proj_w), "proj_bT": column(L0_tok_proj_b, KC),
        "fus_w": chunks(L0_tok_fus_w, 2 * KC), "fus_b": row(L0_tok_fus_b),
        "ln_g": row(L0_tok_ln_g), "ln_b": row(L0_tok_ln_b),
        "wq": chunks(L0_attn_Wq, KC), "wk": chunks(L0_attn_Wk, KC), "wv": chunks(L0_attn_Wv, KC),
        "wo": chunks(np.asarray(L0_attn_Wo).reshape(H * K, D), HD),
        "bqT": column(L0_attn_bq, HD), "bkT": column(L0_attn_bk, HD), "bvT": column(L0_attn_bv, HD),
        "bo": row(L0_attn_bo), "gamma1": row(L0_attn_gamma), "beta1": row(L0_attn_beta),
        "wg": chunks(L0_ffn_wg, KC), "bg": row(L0_ffn_bg),
        "w1": chunks(np.asarray(L0_ffn_w1).transpose(1, 0, 2), KC), "b1T": column(L0_ffn_b1, NJ),
        "w2": chunks(np.asarray(L0_ffn_w2).reshape(E * FP, D), NJ), "b2": lay(L0_ffn_b2),
        "gamma2": row(L0_ffn_gamma), "beta2": row(L0_ffn_beta),
    }
    s = np.arange(P)
    arrays["ident"] = np.eye(P, dtype=np.float32)
    arrays["band"] = (abs(s[:, None] - s[None]) <= 1).astype(np.float32)
    arrays["iota"] = np.tile(np.arange(V, dtype=np.float32), (P, 1))
    arrays["countdown"] = np.tile(np.arange(E, 0, -1, dtype=np.float32), (P, 1))
    expert_of = np.zeros((P, NJ, P), np.float16)
    for j in range(NJ):
        for c in range(P):
            expert_of[(j * P + c) // FP, j, c] = MASK_BIG
    arrays["expert_of"] = expert_of

    nc = bacc.Bacc("TRN2", target_bir_lowering=False, num_devices=1)
    aps = {}
    for name, (shape, dt) in INPUTS.items():
        arrays["in_" + name] = arrays.pop(name)
        aps[name] = nc.dram_tensor("in_" + name, shape, dt, kind="ExternalInput").ap()
    out = nc.dram_tensor("out", [B, S, D], F32, kind="ExternalOutput").ap()
    program(nc, aps, out)
    r = run_bass_kernel_spmd(nc, [arrays], core_ids=[0])
    return r.results[0]["out"]
```
